# Optimizing a Trainium2 kernel written in Bass

```python
import numpy as np
import jax
import jax.numpy as jnp

def _softmax(x, axis=-1):
    return jax.nn.softmax(x, axis=axis)
def _gelu(x):
    return jax.nn.gelu(x, approximate=True)
def _silu(x):
    return jax.nn.silu(x)
def _sigmoid(x):
    return jax.nn.sigmoid(x)
def _layernorm(x, axis=-1, eps=1e-5):
    m = jnp.mean(x, axis=axis, keepdims=True)
    v = jnp.var(x, axis=axis, keepdims=True)
    return (x - m) / jnp.sqrt(v + eps)
def _scatter_add(tgt, idx, src, axis=0):
    return tgt.at[idx].add(src)
def _segment_sum(src, seg, n):
    return jax.ops.segment_sum(src, seg, n)

kernel_name = 'mk_conv_seq_d1_conv_nhwc96_03c348'

def setup_inputs(seed: int = 0):
    np.random.seed(seed)
    _w = jnp.asarray
    def _rec_inputs():
        import jax
        import jax.numpy as jnp
        _gk = jax.random.key(seed)
        x = 0.0001462 + 1 * jax.random.normal(jax.random.fold_in(_gk, 1), (128, 55, 55, 96), jnp.float32)
        return x
    x = _rec_inputs()
    def _L0_conv_setup():
        import jax, jax.numpy as jnp
        import numpy as np
        from jax import lax

        def _make_kernel():
            n = 5
            k = np.zeros((96, n, n), dtype=np.float32)
            k[10] = np.array([[0, 0, 1, 0, 0], [0, 0, 1, 0, 0], [-1, -1, 0, -1, -1], [0, 0, 1, 0, 0], [0, 0, 1, 0, 0]], np.float32) / 8.0
            k[5] = np.array([[0, 0, -1, 0, 0], [0, 0, -1, 0, 0], [1, 1, 0, 1, 1], [0, 0, -1, 0, 0], [0, 0, -1, 0, 0]], np.float32) / 8.0
            diag = np.array([[1, 0, 0, 0, -1], [0, 1, 0, -1, 0], [0, 0, 0, 0, 0], [0, -1, 0, 1, 0], [-1, 0, 0, 0, 1]], np.float32) / 8.0
            k[54] = diag
            k[67] = diag
            return jnp.asarray(k)
        key = jax.random.key(seed)
        x = jax.random.normal(key, (128, 55, 55, 96), dtype=jnp.float32)
        kernel = _make_kernel()
        return {'x': x, 'kernel': kernel}
    _L0_conv_all = _L0_conv_setup()
    _L0_conv_in = {k: v for k, v in _L0_conv_all.items() if k in ('kernel', )}
    del _L0_conv_all

    return {
        "x": x,
        "L0_conv_kernel": _L0_conv_in["kernel"],
    }

def reference(x, L0_conv_kernel):
    import jax
    import jax.numpy as jnp
    def _L0_conv_ref(x, kernel):
        import jax, jax.numpy as jnp
        import numpy as np
        from jax import lax

        def _make_kernel():
            n = 5
            k = np.zeros((96, n, n), dtype=np.float32)
            k[10] = np.array([[0, 0, 1, 0, 0], [0, 0, 1, 0, 0], [-1, -1, 0, -1, -1], [0, 0, 1, 0, 0], [0, 0, 1, 0, 0]], np.float32) / 8.0
            k[5] = np.array([[0, 0, -1, 0, 0], [0, 0, -1, 0, 0], [1, 1, 0, 1, 1], [0, 0, -1, 0, 0], [0, 0, -1, 0, 0]], np.float32) / 8.0
            diag = np.array([[1, 0, 0, 0, -1], [0, 1, 0, -1, 0], [0, 0, 0, 0, 0], [0, -1, 0, 1, 0], [-1, 0, 0, 0, 1]], np.float32) / 8.0
            k[54] = diag
            k[67] = diag
            return jnp.asarray(k)
        ch = x.shape[-1]
        k = jnp.transpose(kernel, (1, 2, 0))[:, :, None, :]
        y = lax.conv_general_dilated(x, k, window_strides=(1, 1), padding='SAME', dimension_numbers=('NHWC', 'HWIO', 'NHWC'), feature_group_count=ch)
        return x + y

    def _gn(v, G=32, eps=1e-5):
        B_, H_, W_, C_ = v.shape
        g = v.reshape(B_, H_, W_, G, C_ // G)
        m = jnp.mean(g, axis=(1, 2, 4), keepdims=True)
        s = jnp.var(g, axis=(1, 2, 4), keepdims=True)
        return ((g - m) / jnp.sqrt(s + eps)).reshape(v.shape)

    def _ln_c(v, eps=1e-6):
        m = jnp.mean(v, axis=-1, keepdims=True)
        s = jnp.var(v, axis=-1, keepdims=True)
        return (v - m) / jnp.sqrt(s + eps)

    def _ln_t(v, eps=1e-5):
        m = jnp.mean(v, axis=-1, keepdims=True)
        s = jnp.var(v, axis=-1, keepdims=True)
        return (v - m) / jnp.sqrt(s + eps)

    def _to_tokens(v):
        B_, H_, W_, C_ = v.shape
        return v.reshape(B_, H_ * W_, C_)
    def _from_tokens(t, like):
        return t.reshape(like.shape)

    x = _L0_conv_ref(x, L0_conv_kernel)
    return x


_drawn_inputs = setup_inputs


def setup_inputs(seed=0):
    import zlib

    import numpy as np

    out = dict(_drawn_inputs(seed))
    spreads = {}
    factors = {}
    for name, (base, spread) in spreads.items():
        noise = np.random.default_rng([zlib.crc32(name.encode()), seed]).standard_normal(out[name].shape)
        drawn = base * np.exp(spread * noise) if base else spread * noise
        out[name] = jnp.asarray(drawn.astype(out[name].dtype))
    for name, factor in factors.items():
        out[name] = (out[name] * factor).astype(out[name].dtype)
    return out
```

```python
from contextlib import ExitStack

import numpy as np

import concourse.bass as bass
from concourse import mybir

F32 = mybir.dt.float32
F32R = mybir.dt.float32r
ALU = mybir.AluOpType
ACT = mybir.ActivationFunctionType

IMAGES, HEIGHT, WIDTH, CHANNELS = 128, 55, 55, 96
TAPS = 5
HALO = TAPS // 2
P = 128

STRIP_IN = 32
STRIP_OUT = STRIP_IN - 2 * HALO
BLOCK = P // STRIP_IN
CHAIN_OUT = 2 * WIDTH + HALO
OUT_BLOCKS = CHAIN_OUT // BLOCK
IN_BLOCKS = OUT_BLOCKS + 1
OUT_PARTS = BLOCK * STRIP_OUT
IN_COLS = IN_BLOCKS * IMAGES
OUT_COLS = OUT_BLOCKS * IMAGES
LOWER_ROW = HEIGHT - STRIP_OUT
assert BLOCK + 2 * HALO <= 2 * BLOCK and CHAIN_OUT % BLOCK == 0 and 2 * STRIP_OUT >= HEIGHT

ALL_BLOCKS = 3 * BLOCK - 1
ZERO_BLOCKS = BLOCK - 1
TAP_BLOCKS = TAPS + 1
BAND_COLS = TAP_BLOCKS * STRIP_IN
TAP_COLS = TAP_BLOCKS * STRIP_OUT
PAD = STRIP_IN - 1
FILTER_LEN = BAND_COLS + STRIP_IN
CENTRE = PAD + STRIP_IN * HALO + HALO
W_COLS = 2 * OUT_PARTS
HIGH, LOW = range(2)

BANK = 512
CHUNK = BANK
GROUPS = ((0, 2), (2, 4), (4, 7))
BANKS = GROUPS[-1][1]
assert CHUNK * BANKS == OUT_COLS
SPLIT_BANK = 4
PIECE_GROUPS = ((0, 1), (2,))
PIECE_IN = ((0, SPLIT_BANK * CHUNK + IMAGES), (SPLIT_BANK * CHUNK + IMAGES, IN_COLS))
PIECE_OUT = ((0, SPLIT_BANK * CHUNK), (SPLIT_BANK * CHUNK, OUT_COLS))
PIECES = 2

PER_TURN = 4
TURNS = CHANNELS // PER_TURN
SLOTS = 2
Y_SLOTS = 2


def wait_reuse(engine, semaphore, count):
    if not (isinstance(count, int) and count == 0):
        engine.wait_ge(semaphore, count)


def uses(turn, k, slots):
    return turn * (PER_TURN // slots) + k // slots


def build(nc, x, filters, out):
    with ExitStack() as ctx:
        def sbuf(name, shape, dt):
            return ctx.enter_context(nc.sbuf_tensor(name, shape, dt))

        def sems(name, count):
            return [ctx.enter_context(nc.semaphore(f"{name}{i}")) for i in range(count)]

        x_in = [sbuf(f"x_in{i}", [P, IN_COLS], F32) for i in range(PER_TURN)]
        x_high = [sbuf(f"x_high{i}", [P, IN_COLS], F32R) for i in range(SLOTS)]
        x_low = [sbuf(f"x_low{i}", [P, IN_COLS], F32R) for i in range(SLOTS)]
        y_out = [sbuf(f"y_out{i}", [OUT_PARTS, OUT_COLS], F32) for i in range(Y_SLOTS)]
        weights = [sbuf(f"weights{i}", [P, 2, W_COLS], F32R) for i in range(SLOTS)]
        band_in = sbuf("band_in", [P, BAND_COLS], F32)
        band = sbuf("band", [P, 2, ALL_BLOCKS * STRIP_OUT], F32R)
        taps_of_band = slice(ZERO_BLOCKS * STRIP_OUT, (ZERO_BLOCKS + TAP_BLOCKS) * STRIP_OUT)
        band_rest = sbuf("band_rest", [P, TAP_COLS], F32)
        residual = sbuf("residual", [P, TAP_COLS], F32)
        psum = ctx.enter_context(nc.psum_tensor("sums", [P, BANKS, BANK], F32))

        residual_zeroed, residual_ready, edges_zeroed, band_zeroed, band_loaded, band_step = (
            sems(n, 1)[0] for n in ("residual_zeroed", "residual_ready", "edges_zeroed", "band_zeroed",
                                    "band_loaded", "band_step"))
        x_loaded = sems("x_loaded", PER_TURN)
        high_ready = sems("high_ready", SLOTS)
        low_ready = sems("low_ready", SLOTS)
        weights_ready = sems("weights_ready", SLOTS)
        sums_done = [sems(f"sums_done{i}_", len(GROUPS)) for i in range(SLOTS)]
        products_done = [done[-1] for done in sums_done]
        banks_empty = sems("banks_empty", len(GROUPS))
        y_stored = [sems(f"y_stored{i}_", PIECES) for i in range(Y_SLOTS)]

        bands = bass.AP(tensor=filters.tensor, offset=0,
                        ap=[[FILTER_LEN, CHANNELS], [1, STRIP_IN], [1, BAND_COLS]])

        def by_block(t, rows):
            return t.rearrange("k (b r) -> k b r", r=rows)

        block = ctx.enter_context(nc.Block())

        @block.sync
        def _(sp):
            def load_band(turn):
                wait_reuse(sp, band_step, 3 * turn)
                sp.dma_start(band_in[:, :], bands[bass.ds(turn * PER_TURN, PER_TURN), :, :]).then_inc(band_loaded, 16)

            def load_x(turn, k):
                if not (isinstance(turn, int) and turn == 0):
                    sp.wait_ge(low_ready[k % SLOTS], PIECES * (uses(turn - 1, k, SLOTS) + 1))
                for parts, cols in ((slice(0, P // 2), slice(IMAGES, IN_COLS)), (slice(P // 2, P), slice(0, OUT_COLS))):
                    sp.dma_start(x_in[k][parts, cols],
                                 x[bass.ds(turn * PER_TURN + k, 1), parts, :].rearrange("c p n -> (c p) n")
                                 ).then_inc(x_loaded[k], 16)

            def store_y(turn, k, piece):
                for g in PIECE_GROUPS[piece]:
                    sp.wait_ge(banks_empty[g], turn * PER_TURN + k + 1)
                cols = slice(*PIECE_OUT[piece])
                sp.dma_start(out[bass.ds(turn * PER_TURN + k, 1), :, cols].rearrange("c p n -> (c p) n"),
                             y_out[k % Y_SLOTS][:, cols]).then_inc(y_stored[k % Y_SLOTS][piece], 16)

            load_band(0)
            for k in range(PER_TURN):
                load_x(0, k)
            with sp.Fori(0, TURNS - 1) as turn:
                load_band(turn + 1)
                for k in range(PER_TURN):
                    load_x(turn + 1, k)
                    for piece in range(PIECES):
                        store_y(turn, k, piece)
            for k in range(PER_TURN):
                for piece in range(PIECES):
                    store_y(TURNS - 1, k, piece)
            for slot in y_stored:
                for semaphore in slot:
                    sp.wait_ge(semaphore, 16 * CHANNELS // Y_SLOTS)

        @block.gpsimd
        def _(pool):
            pool.memset(residual[:, :], 0.0).then_inc(residual_zeroed, 1)
            pool.wait_ge(residual_zeroed, 1)
            for k in range(PER_TURN):
                quadrant = by_block(residual[k * STRIP_IN:(k + 1) * STRIP_IN, :], STRIP_OUT)
                pool.affine_select(out=quadrant, in_=quadrant, compare_op=ALU.not_equal, fill=1.0,
                                   base=STRIP_IN - STRIP_OUT - CENTRE,
                                   pattern=[[STRIP_IN, TAP_BLOCKS], [1, STRIP_OUT]],
                                   channel_multiplier=1).then_inc(residual_ready, 1)

        @block.scalar
        def _(act):
            def split_high(turn, k, piece):
                a, b = PIECE_IN[piece]
                if piece == 0:
                    act.wait_ge(x_loaded[k], 2 * 16 * (turn + 1))
                    wait_reuse(act, products_done[k % SLOTS], uses(turn, k, SLOTS))
                act.activation(x_high[k % SLOTS][:, a:b], x_in[k][:, a:b], ACT.Copy).then_inc(high_ready[k % SLOTS], 1)

            def empty_banks(turn, k, g):
                act.wait_ge(sums_done[k % SLOTS][g], uses(turn, k, SLOTS) + 1)
                for piece in range(PIECES):
                    if g == PIECE_GROUPS[piece][0]:
                        wait_reuse(act, y_stored[k % Y_SLOTS][piece], 16 * uses(turn, k, Y_SLOTS))
                a, b = GROUPS[g]
                act.activation(y_out[k % Y_SLOTS][:, a * CHUNK:b * CHUNK],
                               psum[0:OUT_PARTS, a:b, :].rearrange("p b n -> p (b n)"),
                               ACT.Copy).then_inc(banks_empty[g], 1)

            def channel(turn, k, last=False):
                following = (turn, k + 1) if k + 1 < PER_TURN else (turn + 1, 0)
                if not last:
                    split_high(*following, 0)
                empty_banks(turn, k, 0)
                if not last:
                    split_high(*following, 1)
                empty_banks(turn, k, 1)
                empty_banks(turn, k, 2)

            act.wait_ge(edges_zeroed, 2 * PER_TURN)
            split_high(0, 0, 0)
            split_high(0, 0, 1)
            for k in range(PER_TURN):
                channel(0, k)
            with act.Fori(1, TURNS - 1) as turn:
                for k in range(PER_TURN):
                    channel(turn, k)
            for k in range(PER_TURN):
                channel(TURNS - 1, k, last=k == PER_TURN - 1)

        @block.vector
        def _(dve):
            def split_bands(turn):
                taps = by_block(band_in[:, :], STRIP_IN)[:, :, STRIP_IN - STRIP_OUT:]
                dve.wait_ge(band_loaded, 16 * (turn + 1))
                for slot in range(SLOTS):
                    wait_reuse(dve, weights_ready[slot], BLOCK * uses(turn, 0, SLOTS))
                dve.tensor_tensor(by_block(band[:, HIGH, taps_of_band], STRIP_OUT), taps, by_block(residual[:, :], STRIP_OUT),
                                  ALU.add).then_inc(band_step, 1)
                dve.wait_ge(band_step, 3 * turn + 1)
                dve.tensor_tensor(band_rest[:, :], band[:, HIGH, taps_of_band].bitcast(F32), residual[:, :],
                                  ALU.subtract).then_inc(band_step, 1)
                dve.wait_ge(band_step, 3 * turn + 2)
                dve.tensor_tensor(by_block(band[:, LOW, taps_of_band], STRIP_OUT), taps, by_block(band_rest[:, :], STRIP_OUT),
                                  ALU.subtract).then_inc(band_step, 1)
                dve.wait_ge(band_step, 3 * turn + 3)

            def place_weights(turn, k):
                wait_reuse(dve, products_done[k % SLOTS], uses(turn, k, SLOTS))
                for q in range(BLOCK):
                    dve.tensor_copy(weights[k % SLOTS][q * STRIP_IN:(q + 1) * STRIP_IN, :, :],
                                    band[k * STRIP_IN:(k + 1) * STRIP_IN, :, q * STRIP_OUT:q * STRIP_OUT + W_COLS]
                                    .bitcast(F32)).then_inc(weights_ready[k % SLOTS], 1)

            def split_low(turn, k, piece):
                a, b = PIECE_IN[piece]
                slot = k % SLOTS
                dve.wait_ge(high_ready[slot], PIECES * uses(turn, k, SLOTS) + piece + 1)
                dve.tensor_tensor(x_low[slot][:, a:b], x_in[k][:, a:b], x_high[slot][:, a:b].bitcast(F32),
                                  ALU.subtract).then_inc(low_ready[slot], 1)

            def split_turn(turn):
                split_bands(turn)
                for k in range(PER_TURN):
                    place_weights(turn, k)
                    for piece in range(PIECES):
                        split_low(turn, k, piece)

            for k in range(PER_TURN):
                dve.memset(x_in[k][0:P // 2, 0:IMAGES], 0.0).then_inc(edges_zeroed, 1)
                dve.memset(x_in[k][P // 2:P, OUT_COLS:IN_COLS], 0.0).then_inc(edges_zeroed, 1)
            dve.wait_ge(edges_zeroed, 2 * PER_TURN)
            dve.memset(band[:, :, :].bitcast(F32), 0.0).then_inc(band_zeroed, 1)
            dve.wait_ge(band_zeroed, 1)
            dve.wait_ge(residual_ready, PER_TURN)
            split_turn(0)
            with dve.Fori(1, TURNS) as turn:
                split_turn(turn)

        @block.tensor
        def _(pe):
            parts = [(w, v) for w, v in ((HIGH, x_low), (LOW, x_high), (HIGH, x_high))]

            def channel(turn, k):
                slot = k % SLOTS
                pe.wait_ge(weights_ready[slot], BLOCK * (uses(turn, k, SLOTS) + 1))
                for piece in range(PIECES):
                    pe.wait_ge(low_ready[slot], PIECES * uses(turn, k, SLOTS) + piece + 1)
                    for g in PIECE_GROUPS[piece]:
                        wait_reuse(pe, banks_empty[g], turn * PER_TURN + k)
                        for bank in range(*GROUPS[g]):
                            products = [(w, v, side) for w, v in parts for side in range(2)]
                            for n, (w, v, side) in enumerate(products):
                                first = bank * CHUNK + side * IMAGES
                                product = pe.matmul(psum[0:OUT_PARTS, bank, :],
                                                    weights[slot][:, w, side * OUT_PARTS:(side + 1) * OUT_PARTS],
                                                    v[slot][:, first:first + CHUNK],
                                                    start=n == 0, stop=n == len(products) - 1)
                        product.then_inc(sums_done[slot][g], 1)

            for k in range(PER_TURN):
                channel(0, k)
            with pe.Fori(1, TURNS) as turn:
                for k in range(PER_TURN):
                    channel(turn, k)


def lay_out_input(x):
    chain = np.zeros((CHANNELS, IN_BLOCKS * BLOCK, STRIP_IN, IMAGES), x.dtype)
    pixels = x.transpose(3, 2, 1, 0)
    upper_rows = STRIP_IN - HALO
    chain[:, HALO:HALO + WIDTH, HALO:] = pixels[:, :, :upper_rows]
    lower = HALO + WIDTH + HALO
    lower_rows = HEIGHT - (LOWER_ROW - HALO)
    chain[:, lower:lower + WIDTH, :lower_rows] = pixels[:, :, LOWER_ROW - HALO:]
    chain = chain.reshape(CHANNELS, IN_BLOCKS, BLOCK, STRIP_IN, IMAGES)
    parts = chain.transpose(0, 2, 3, 1, 4)
    parts = np.concatenate([parts[:, :BLOCK // 2, :, 1:], parts[:, BLOCK // 2:, :, :-1]], axis=1)
    return np.ascontiguousarray(parts).reshape(CHANNELS, P, OUT_COLS)


def lay_out_filters(taps):
    row = np.zeros((CHANNELS, FILTER_LEN), taps.dtype)
    for dj in range(TAPS):
        at = PAD + STRIP_IN * dj
        row[:, at:at + TAPS] = taps[:, :, dj]
    return row


def lay_out_output(y):
    y = y.reshape(CHANNELS, BLOCK, STRIP_OUT, OUT_BLOCKS, IMAGES)[:, ::-1, ::-1]
    chain = y.transpose(0, 3, 1, 2, 4).reshape(CHANNELS, CHAIN_OUT, STRIP_OUT, IMAGES)
    out = np.empty((IMAGES, HEIGHT, WIDTH, CHANNELS), y.dtype)
    out[:, :STRIP_OUT] = chain[:, :WIDTH].transpose(3, 2, 1, 0)
    out[:, LOWER_ROW:] = chain[:, WIDTH + HALO:].transpose(3, 2, 1, 0)
    return out


def kernel(x, L0_conv_kernel):
    import concourse.bacc as bacc
    from concourse.bass_utils import run_bass_kernel_spmd

    arrays = {"x": lay_out_input(np.asarray(x)), "filters": lay_out_filters(np.asarray(L0_conv_kernel))}
    nc = bacc.Bacc("TRN2", target_bir_lowering=False, num_devices=1)
    ins = [nc.dram_tensor(name, a.shape, mybir.dt.from_np(a.dtype), kind="ExternalInput").ap()
           for name, a in arrays.items()]
    out = nc.dram_tensor("y", (CHANNELS, OUT_PARTS, OUT_COLS), F32, kind="ExternalOutput").ap()
    build(nc, *ins, out)
    result = run_bass_kernel_spmd(nc, [arrays], core_ids=[0])
    return lay_out_output(result.results[0]["y"])
```

```python
from contextlib import ExitStack

import numpy as np

import concourse.bass as bass
from concourse import mybir

F32 = mybir.dt.float32
F32R = mybir.dt.float32r
ALU = mybir.AluOpType
ACT = mybir.ActivationFunctionType

IMAGES, HEIGHT, WIDTH, CHANNELS = 128, 55, 55, 96
TAPS = 5
HALO = TAPS // 2
P = 128

STRIP_IN = 32
STRIP_LOAD = STRIP_IN - HALO
STRIP_OUT = STRIP_LOAD
STRIP_KEEP = STRIP_OUT - HALO
BLOCK = P // STRIP_IN
CHAIN_OUT = 2 * WIDTH + HALO
OUT_BLOCKS = CHAIN_OUT // BLOCK
IN_BLOCKS = OUT_BLOCKS + 1
OUT_PARTS = BLOCK * STRIP_OUT
KEEP_PARTS = BLOCK * STRIP_KEEP
IN_COLS = IN_BLOCKS * IMAGES
OUT_COLS = OUT_BLOCKS * IMAGES
STRIP_COLS = OUT_COLS // 2
assert BLOCK + 2 * HALO <= 2 * BLOCK and CHAIN_OUT % (2 * BLOCK) == 0 and 2 * STRIP_KEEP >= HEIGHT

ALL_BLOCKS = 3 * BLOCK - 1
ZERO_BLOCKS = BLOCK - 1
TAP_BLOCKS = TAPS + 1
BAND_COLS = TAP_BLOCKS * STRIP_IN
TAP_COLS = TAP_BLOCKS * STRIP_OUT
PAD = STRIP_IN - 1
FILTER_LEN = BAND_COLS + STRIP_IN
CENTRE = PAD + STRIP_IN * HALO + HALO
W_COLS = 2 * OUT_PARTS
HIGH, LOW = range(2)
PLACE_STEPS = 2 * BLOCK

BANK = 512
CHUNK = BANK
GROUPS = ((0, 2), (2, 4), (4, 7))
BANKS = GROUPS[-1][1]
assert CHUNK * BANKS == OUT_COLS
SPLIT_BANK = 4
PIECE_GROUPS = ((0, 1), (2,))
PIECE_IN = ((0, SPLIT_BANK * CHUNK + IMAGES), (SPLIT_BANK * CHUNK + IMAGES, IN_COLS))
PIECES = 2
UPPER, LOWER = range(2)
STRIPS = 2
STRIP_GROUPS = ((0, 1), (1, 2))
STRIP_FIRST = (OUT_PARTS - KEEP_PARTS, 0)

PER_TURN = 4
TURNS = CHANNELS // PER_TURN
SLOTS = 2
Y_SLOTS = 2


def wait_reuse(engine, semaphore, count):
    if not (isinstance(count, int) and count == 0):
        engine.wait_ge(semaphore, count)


def uses(turn, k, slots):
    return turn * (PER_TURN // slots) + k // slots


def build(nc, x, zeros, filters, out):
    with ExitStack() as ctx:
        def sbuf(name, shape, dt):
            return ctx.enter_context(nc.sbuf_tensor(name, shape, dt))

        def sems(name, count):
            return [ctx.enter_context(nc.semaphore(f"{name}{i}")) for i in range(count)]

        x_in = [sbuf(f"x_in{i}", [P, IN_COLS], F32) for i in range(PER_TURN)]
        x_high = [sbuf(f"x_high{i}", [P, IN_COLS], F32R) for i in range(SLOTS)]
        x_low = [sbuf(f"x_low{i}", [P, IN_COLS], F32R) for i in range(SLOTS)]
        y_out = [sbuf(f"y_out{i}", [OUT_PARTS, OUT_COLS], F32) for i in range(Y_SLOTS)]
        weights = [sbuf(f"weights{i}", [P, 2, W_COLS], F32R) for i in range(SLOTS)]
        band_in = sbuf("band_in", [P, BAND_COLS], F32)
        band = sbuf("band", [P, 2, ALL_BLOCKS * STRIP_OUT], F32R)
        taps_of_band = slice(ZERO_BLOCKS * STRIP_OUT, (ZERO_BLOCKS + TAP_BLOCKS) * STRIP_OUT)
        band_rest = sbuf("band_rest", [P, TAP_COLS], F32)
        residual = sbuf("residual", [P, TAP_COLS], F32)
        warm = sbuf("warm", [P, 1], F32)
        psum = ctx.enter_context(nc.psum_tensor("sums", [P, BANKS, BANK], F32))

        (warm_zeroed, warmed, residual_zeroed, residual_ready, edges_zeroed, band_zeroed, band_loaded, band_step,
         first_loaded) = (sems(n, 1)[0] for n in (
             "warm_zeroed", "warmed", "residual_zeroed", "residual_ready", "edges_zeroed", "band_zeroed",
             "band_loaded", "band_step", "first_loaded"))
        zero_rows = sems("zero_rows", PER_TURN)
        x_loaded = sems("x_loaded", PER_TURN)
        high_ready = sems("high_ready", SLOTS)
        low_ready = sems("low_ready", SLOTS)
        weights_ready = sems("weights_ready", SLOTS)
        sums_done = [sems(f"sums_done{i}_", len(GROUPS)) for i in range(SLOTS)]
        products_done = [done[-1] for done in sums_done]
        banks_empty = sems("banks_empty", len(GROUPS))
        y_stored = [sems(f"y_stored{i}_", STRIPS) for i in range(Y_SLOTS)]

        bands = bass.AP(tensor=filters.tensor, offset=0,
                        ap=[[FILTER_LEN, CHANNELS], [1, STRIP_IN], [1, BAND_COLS]])

        def by_block(t, rows):
            return t.rearrange("k (b r) -> k b r", r=rows)

        def loaded_cols(q):
            return slice(IMAGES, IN_COLS) if q < HALO else slice(0, OUT_COLS)

        def load_zero_rows(engine, k):
            for q in range(BLOCK):
                engine.dma_start(x_in[k][q * STRIP_IN:q * STRIP_IN + HALO, loaded_cols(q)],
                                 zeros).then_inc(zero_rows[k], 16)

        def load_columns(engine, quadrants, turn, k, start, end, loaded):
            for q in quadrants:
                cols = loaded_cols(q)
                a, b = max(start, cols.start), min(end, cols.stop)
                engine.dma_start(x_in[k][q * STRIP_IN + HALO:(q + 1) * STRIP_IN, a:b],
                                 x[bass.ds(turn * PER_TURN + k, 1), q * STRIP_LOAD:(q + 1) * STRIP_LOAD,
                                   a - cols.start:b - cols.start].rearrange("c p n -> (c p) n")
                                 ).then_inc(loaded, 16)

        def load_x(engine, quadrants, turn, k):
            if not (isinstance(turn, int) and turn == 0):
                engine.wait_ge(low_ready[k % SLOTS], PIECES * (uses(turn - 1, k, SLOTS) + 1))
            load_columns(engine, quadrants, turn, k, 0, IN_COLS, x_loaded[k])

        block = ctx.enter_context(nc.Block())

        @block.sync
        def _(sp):
            def load_band(turn):
                wait_reuse(sp, band_step, 3 * turn)
                sp.dma_start(band_in[:, :], bands[bass.ds(turn * PER_TURN, PER_TURN), :, :]).then_inc(band_loaded, 16)

            def store_y(turn, k, strip):
                for g in STRIP_GROUPS[strip]:
                    sp.wait_ge(banks_empty[g], turn * PER_TURN + k + 1)
                first, col = STRIP_FIRST[strip], strip * STRIP_COLS
                sp.dma_start(out[bass.ds(turn * PER_TURN + k, 1), strip, :, :].rearrange("c p n -> (c p) n"),
                             y_out[k % Y_SLOTS][first:first + KEEP_PARTS, col:col + STRIP_COLS]
                             ).then_inc(y_stored[k % Y_SLOTS][strip], 16)

            load_columns(sp, range(BLOCK), 0, 0, *PIECE_IN[0], first_loaded)
            load_band(0)
            load_columns(sp, range(BLOCK), 0, 0, *PIECE_IN[1], x_loaded[0])
            for k in range(1, PER_TURN):
                load_x(sp, (0, 1), 0, k)
            with sp.Fori(0, TURNS - 1) as turn:
                load_band(turn + 1)
                for k in range(PER_TURN):
                    load_x(sp, (0, 1), turn + 1, k)
                    for strip in range(STRIPS):
                        store_y(turn, k, strip)
            for k in range(PER_TURN):
                for strip in range(STRIPS):
                    store_y(TURNS - 1, k, strip)
            for slot in y_stored:
                for semaphore in slot:
                    sp.wait_ge(semaphore, 16 * CHANNELS // Y_SLOTS)

        @block.gpsimd
        def _(pool):
            pool.memset(residual[:, :], 0.0).then_inc(residual_zeroed, 1)
            pool.wait_ge(residual_zeroed, 1)
            for k in range(PER_TURN):
                quadrant = by_block(residual[k * STRIP_IN:(k + 1) * STRIP_IN, :], STRIP_OUT)
                pool.affine_select(out=quadrant, in_=quadrant, compare_op=ALU.not_equal, fill=1.0,
                                   base=STRIP_IN - STRIP_OUT - CENTRE,
                                   pattern=[[STRIP_IN, TAP_BLOCKS], [1, STRIP_OUT]],
                                   channel_multiplier=1).then_inc(residual_ready, 1)
            for k in range(1, PER_TURN):
                load_zero_rows(pool, k)

        @block.scalar
        def _(act):
            def split_high(turn, k, piece):
                a, b = PIECE_IN[piece]
                if piece == 0:
                    if isinstance(turn, int) and (turn, k) == (0, 0):
                        act.wait_ge(first_loaded, BLOCK * 16)
                    else:
                        act.wait_ge(x_loaded[k], BLOCK * 16 * (turn + 1))
                    if isinstance(turn, int) and turn == 0:
                        act.wait_ge(zero_rows[k], BLOCK * 16)
                    wait_reuse(act, products_done[k % SLOTS], uses(turn, k, SLOTS))
                elif isinstance(turn, int) and (turn, k) == (0, 0):
                    act.wait_ge(x_loaded[k], BLOCK * 16)
                act.activation(x_high[k % SLOTS][:, a:b], x_in[k][:, a:b], ACT.Copy).then_inc(high_ready[k % SLOTS], 1)

            def empty_banks(turn, k, g):
                act.wait_ge(sums_done[k % SLOTS][g], uses(turn, k, SLOTS) + 1)
                for strip in range(STRIPS):
                    if g in STRIP_GROUPS[strip]:
                        wait_reuse(act, y_stored[k % Y_SLOTS][strip], 16 * uses(turn, k, Y_SLOTS))
                a, b = GROUPS[g]
                act.activation(y_out[k % Y_SLOTS][:, a * CHUNK:b * CHUNK],
                               psum[0:OUT_PARTS, a:b, :].rearrange("p b n -> p (b n)"),
                               ACT.Copy).then_inc(banks_empty[g], 1)

            def channel(turn, k, last_turn=False):
                last = last_turn and k == PER_TURN - 1
                following = (turn, k + 1) if k + 1 < PER_TURN else (turn + 1, 0)
                if not last:
                    split_high(*following, 0)
                empty_banks(turn, k, 0)
                if not last_turn:
                    load_x(act, (2, 3), turn + 1, k)
                if not last:
                    split_high(*following, 1)
                empty_banks(turn, k, 1)
                empty_banks(turn, k, 2)

            load_zero_rows(act, 0)
            act.wait_ge(warm_zeroed, 1)
            act.activation(warm[:, :], warm[:, :], ACT.Copy).then_inc(warmed, 1)
            act.wait_ge(edges_zeroed, 2 * PER_TURN)
            split_high(0, 0, 0)
            for k in range(1, PER_TURN):
                load_x(act, (2, 3), 0, k)
            split_high(0, 0, 1)
            for k in range(PER_TURN):
                channel(0, k)
            with act.Fori(1, TURNS - 1) as turn:
                for k in range(PER_TURN):
                    channel(turn, k)
            for k in range(PER_TURN):
                channel(TURNS - 1, k, last_turn=True)

        @block.vector
        def _(dve):
            def split_bands(turn):
                taps = by_block(band_in[:, :], STRIP_IN)[:, :, STRIP_IN - STRIP_OUT:]
                dve.wait_ge(band_loaded, 16 * (turn + 1))
                for slot in range(SLOTS):
                    wait_reuse(dve, weights_ready[slot], PLACE_STEPS * uses(turn, 0, SLOTS))
                dve.tensor_tensor(by_block(band[:, HIGH, taps_of_band], STRIP_OUT), taps,
                                  by_block(residual[:, :], STRIP_OUT), ALU.add).then_inc(band_step, 1)
                dve.wait_ge(band_step, 3 * turn + 1)
                dve.tensor_tensor(band_rest[:, :], band[:, HIGH, taps_of_band].bitcast(F32), residual[:, :],
                                  ALU.subtract).then_inc(band_step, 1)
                dve.wait_ge(band_step, 3 * turn + 2)
                dve.tensor_tensor(by_block(band[:, LOW, taps_of_band], STRIP_OUT), taps,
                                  by_block(band_rest[:, :], STRIP_OUT), ALU.subtract).then_inc(band_step, 1)
                dve.wait_ge(band_step, 3 * turn + 3)

            def place_weights(turn, k):
                wait_reuse(dve, products_done[k % SLOTS], uses(turn, k, SLOTS))
                for q in range(BLOCK):
                    for part in (HIGH, LOW):
                        window = band[k * STRIP_IN:(k + 1) * STRIP_IN, part, q * STRIP_OUT:q * STRIP_OUT + W_COLS]
                        target = weights[k % SLOTS][q * STRIP_IN:(q + 1) * STRIP_IN, part, :]
                        dve.tensor_copy(target.rearrange("k (s r c) -> k s c r", s=2, c=BLOCK),
                                        window.bitcast(F32).rearrange("k (s c r) -> k s c r", s=2, c=BLOCK)
                                        ).then_inc(weights_ready[k % SLOTS], 1)

            def split_low(turn, k, piece):
                a, b = PIECE_IN[piece]
                slot = k % SLOTS
                dve.wait_ge(high_ready[slot], PIECES * uses(turn, k, SLOTS) + piece + 1)
                dve.tensor_tensor(x_low[slot][:, a:b], x_in[k][:, a:b], x_high[slot][:, a:b].bitcast(F32),
                                  ALU.subtract).then_inc(low_ready[slot], 1)

            def split_turn(turn):
                split_bands(turn)
                for k in range(PER_TURN):
                    place_weights(turn, k)
                    for piece in range(PIECES):
                        split_low(turn, k, piece)

            dve.memset(warm[:, :], 0.0).then_inc(warm_zeroed, 1)
            for k in range(PER_TURN):
                dve.memset(x_in[k][0:P // 2, 0:IMAGES], 0.0).then_inc(edges_zeroed, 1)
                dve.memset(x_in[k][P // 2:P, OUT_COLS:IN_COLS], 0.0).then_inc(edges_zeroed, 1)
            dve.wait_ge(edges_zeroed, 2 * PER_TURN)
            dve.memset(band[:, :, :].bitcast(F32), 0.0).then_inc(band_zeroed, 1)
            dve.wait_ge(band_zeroed, 1)
            dve.wait_ge(residual_ready, PER_TURN)
            split_turn(0)
            with dve.Fori(1, TURNS) as turn:
                split_turn(turn)

        @block.tensor
        def _(pe):
            parts = [(w, v) for w, v in ((HIGH, x_low), (LOW, x_high), (HIGH, x_high))]

            def channel(turn, k):
                slot = k % SLOTS
                pe.wait_ge(weights_ready[slot], PLACE_STEPS * (uses(turn, k, SLOTS) + 1))
                for piece in range(PIECES):
                    pe.wait_ge(low_ready[slot], PIECES * uses(turn, k, SLOTS) + piece + 1)
                    for g in PIECE_GROUPS[piece]:
                        wait_reuse(pe, banks_empty[g], turn * PER_TURN + k)
                        for bank in range(*GROUPS[g]):
                            products = [(w, v, side) for w, v in parts for side in range(2)]
                            for n, (w, v, side) in enumerate(products):
                                first = bank * CHUNK + side * IMAGES
                                product = pe.matmul(psum[0:OUT_PARTS, bank, :],
                                                    weights[slot][:, w, side * OUT_PARTS:(side + 1) * OUT_PARTS],
                                                    v[slot][:, first:first + CHUNK],
                                                    start=n == 0, stop=n == len(products) - 1)
                        product.then_inc(sums_done[slot][g], 1)

            for k in range(PER_TURN):
                channel(0, k)
            with pe.Fori(1, TURNS) as turn:
                for k in range(PER_TURN):
                    channel(turn, k)


def lay_out_input(x):
    chain = np.zeros((CHANNELS, IN_BLOCKS * BLOCK, STRIP_LOAD, IMAGES), x.dtype)
    pixels = x.transpose(3, 2, 1, 0)
    lower = HALO + WIDTH + HALO
    chain[:, HALO:HALO + WIDTH] = pixels[:, :, :STRIP_LOAD]
    chain[:, lower:lower + WIDTH] = pixels[:, :, HEIGHT - STRIP_LOAD:]
    parts = chain.reshape(CHANNELS, IN_BLOCKS, BLOCK, STRIP_LOAD, IMAGES).transpose(0, 2, 3, 1, 4)
    parts = np.concatenate([parts[:, :HALO, :, 1:], parts[:, HALO:, :, :-1]], axis=1)
    return parts.reshape(CHANNELS, BLOCK * STRIP_LOAD, OUT_COLS)


def lay_out_filters(taps):
    row = np.zeros((CHANNELS, FILTER_LEN), taps.dtype)
    for dj in range(TAPS):
        at = PAD + STRIP_IN * dj
        row[:, at:at + TAPS] = taps[:, :, dj]
    return row


def lay_out_output(y):
    y = y.reshape(CHANNELS, STRIPS, STRIP_KEEP, BLOCK, OUT_BLOCKS // 2, IMAGES)[:, :, ::-1, ::-1]
    columns = y.transpose(5, 1, 2, 4, 3, 0).reshape(IMAGES, STRIPS, STRIP_KEEP, CHAIN_OUT // 2, CHANNELS)
    out = np.empty((IMAGES, HEIGHT, WIDTH, CHANNELS), y.dtype)
    out[:, :STRIP_KEEP] = columns[:, UPPER, :, :WIDTH]
    out[:, HEIGHT - STRIP_KEEP:] = columns[:, LOWER, :, CHAIN_OUT // 2 - WIDTH:]
    return out


def kernel(x, L0_conv_kernel):
    import concourse.bacc as bacc
    from concourse.bass_utils import run_bass_kernel_spmd

    x = lay_out_input(np.asarray(x))
    arrays = {"x": x, "zeros": np.zeros((HALO, OUT_COLS), x.dtype),
              "filters": lay_out_filters(np.asarray(L0_conv_kernel))}
    nc = bacc.Bacc("TRN2", target_bir_lowering=False, num_devices=1)
    ins = [nc.dram_tensor(name, a.shape, mybir.dt.from_np(a.dtype), kind="ExternalInput").ap()
           for name, a in arrays.items()]
    out = nc.dram_tensor("y", (CHANNELS, STRIPS, KEEP_PARTS, STRIP_COLS), F32, kind="ExternalOutput").ap()
    build(nc, *ins, out)
    result = run_bass_kernel_spmd(nc, [arrays], core_ids=[0])
    return lay_out_output(result.results[0]["y"])
```
